# Optimizing a Trainium2 kernel written in Bass

```python
import numpy as np
import jax
import jax.numpy as jnp

def _softmax(x, axis=-1):
    return jax.nn.softmax(x, axis=axis)

def _gelu(x):
    return jax.nn.gelu(x, approximate=True)

def _silu(x):
    return jax.nn.silu(x)

def _sigmoid(x):
    return jax.nn.sigmoid(x)

def _layernorm(x, axis=-1, eps=1e-05):
    m = jnp.mean(x, axis=axis, keepdims=True)
    v = jnp.var(x, axis=axis, keepdims=True)
    return (x - m) / jnp.sqrt(v + eps)

def _scatter_add(tgt, idx, src, axis=0):
    return tgt.at[idx].add(src)

def _segment_sum(src, seg, n):
    return jax.ops.segment_sum(src, seg, n)
kernel_name = 'mk_macaron_d2_jaxref_r8_419d61'

def setup_inputs(seed: int=0):
    np.random.seed(seed)
    _w = jnp.asarray

    def _L0_attn_setup():
        import jax, jax.numpy as jnp
        import numpy as np
        N, S, D_IN, ATTN_DIM, OUT_DIM = (4, 1024, 128, 128, 128)
        key = jax.random.key(seed)
        ks = jax.random.split(key, 6)
        scale_in = 1.0 / np.sqrt(D_IN)
        scale_attn = 1.0 / np.sqrt(ATTN_DIM)
        return {'x': jax.random.normal(ks[0], (N, S, D_IN), dtype=jnp.float32), 'wq': jax.random.normal(ks[1], (D_IN, ATTN_DIM), dtype=jnp.float32) * scale_in, 'bq': jnp.zeros((ATTN_DIM,), dtype=jnp.float32), 'wk': jax.random.normal(ks[2], (D_IN, ATTN_DIM), dtype=jnp.float32) * scale_in, 'bk': jnp.zeros((ATTN_DIM,), dtype=jnp.float32), 'wv': jax.random.normal(ks[3], (D_IN, ATTN_DIM), dtype=jnp.float32) * scale_in, 'bv': jnp.zeros((ATTN_DIM,), dtype=jnp.float32), 'wo': jax.random.normal(ks[4], (ATTN_DIM, OUT_DIM), dtype=jnp.float32) * scale_attn, 'bo': jnp.zeros((OUT_DIM,), dtype=jnp.float32)}
    _L0_attn_in = _L0_attn_setup()

    def _L0_ffn_setup():
        import jax, jax.numpy as jnp
        import numpy as np
        B, S, D, E, H = (2, 128, 128, 16, 256)
        TOP_K = 2
        TEMP = 1.0
        key = jax.random.key(seed)
        ks = jax.random.split(key, 4)
        sc_d = 1.0 / np.sqrt(D)
        sc_h = 1.0 / np.sqrt(H)
        return {'x': jax.random.normal(ks[0], (B, S, D), dtype=jnp.float32), 'Wr': jax.random.normal(ks[1], (D, E), dtype=jnp.float32) * sc_d, 'br': jnp.zeros((E,), dtype=jnp.float32), 'W1': jax.random.normal(ks[2], (E, D, H), dtype=jnp.float32) * sc_d, 'b1': jnp.zeros((E, H), dtype=jnp.float32), 'W2': jax.random.normal(ks[3], (E, H, D), dtype=jnp.float32) * sc_h, 'b2': jnp.zeros((E, D), dtype=jnp.float32)}
    _L0_ffn_in = _L0_ffn_setup()

    def _L1_attn_setup():
        import jax, jax.numpy as jnp
        import numpy as np
        NUM_HEADS = 16
        HIDDEN = 128
        HEAD_DIM = HIDDEN // NUM_HEADS
        B, L = (2, 256)
        key = jax.random.key(seed)
        ks = jax.random.split(key, 5)
        scale = 1.0 / np.sqrt(HIDDEN)
        return {'x': jax.random.normal(ks[0], (B, L, HIDDEN), dtype=jnp.float32), 'Wq': jax.random.normal(ks[1], (HIDDEN, HIDDEN), dtype=jnp.float32) * scale, 'Wk': jax.random.normal(ks[2], (HIDDEN, HIDDEN), dtype=jnp.float32) * scale, 'Wv': jax.random.normal(ks[3], (HIDDEN, HIDDEN), dtype=jnp.float32) * scale, 'Wo': jax.random.normal(ks[4], (HIDDEN, HIDDEN), dtype=jnp.float32) * scale}
    _L1_attn_in = _L1_attn_setup()

    def _L1_ffn_setup():
        import jax, jax.numpy as jnp
        import numpy as np
        B, S, H, E = (2, 256, 128, 16)
        key = jax.random.key(seed)
        k0, k1, k2, k3 = jax.random.split(key, 4)
        tokens = jax.random.normal(k0, (B, S, H), dtype=jnp.float32)
        gate_w = jax.random.normal(k1, (E, H), dtype=jnp.float32) * H ** (-0.5)
        expert_w = jax.random.normal(k2, (E, H, H), dtype=jnp.float32) * H ** (-0.5)
        expert_b = jax.random.normal(k3, (E, H), dtype=jnp.float32) * 0.01
        return {'tokens': tokens, 'gate_w': gate_w, 'expert_w': expert_w, 'expert_b': expert_b}
    _L1_ffn_in = _L1_ffn_setup()
    _d = {'L0_attn_x': _L0_attn_in['x'], 'L0_attn_wq': _L0_attn_in['wq'], 'L0_attn_bq': _L0_attn_in['bq'], 'L0_attn_wk': _L0_attn_in['wk'], 'L0_attn_bk': _L0_attn_in['bk'], 'L0_attn_wv': _L0_attn_in['wv'], 'L0_attn_bv': _L0_attn_in['bv'], 'L0_attn_wo': _L0_attn_in['wo'], 'L0_attn_bo': _L0_attn_in['bo'], 'L0_ffn_Wr': _L0_ffn_in['Wr'], 'L0_ffn_br': _L0_ffn_in['br'], 'L0_ffn_W1': _L0_ffn_in['W1'], 'L0_ffn_b1': _L0_ffn_in['b1'], 'L0_ffn_W2': _L0_ffn_in['W2'], 'L0_ffn_b2': _L0_ffn_in['b2'], 'L1_attn_Wq': _L1_attn_in['Wq'], 'L1_attn_Wk': _L1_attn_in['Wk'], 'L1_attn_Wv': _L1_attn_in['Wv'], 'L1_attn_Wo': _L1_attn_in['Wo'], 'L1_ffn_gate_w': _L1_ffn_in['gate_w'], 'L1_ffn_expert_w': _L1_ffn_in['expert_w'], 'L1_ffn_expert_b': _L1_ffn_in['expert_b']}
    _x0 = _d['L0_attn_x']
    _d['L0_attn_x'] = jax.random.normal(jax.random.fold_in(jax.random.key(seed), 1), (8, 256, 128), dtype=_x0.dtype)
    del _x0
    return _d

def reference(L0_attn_x, L0_attn_wq, L0_attn_bq, L0_attn_wk, L0_attn_bk, L0_attn_wv, L0_attn_bv, L0_attn_wo, L0_attn_bo, L0_ffn_Wr, L0_ffn_br, L0_ffn_W1, L0_ffn_b1, L0_ffn_W2, L0_ffn_b2, L1_attn_Wq, L1_attn_Wk, L1_attn_Wv, L1_attn_Wo, L1_ffn_gate_w, L1_ffn_expert_w, L1_ffn_expert_b):

    def _L0_attn_ref(x, wq, bq, wk, bk, wv, bv, wo, bo):
        import jax, jax.numpy as jnp
        import numpy as np
        N, S, D_IN, ATTN_DIM, OUT_DIM = (4, 1024, 128, 128, 128)
        query = x @ wq + bq
        key_ = x @ wk + bk
        value = x @ wv + bv
        Q = jax.nn.elu(query) + 1.0
        K = jax.nn.elu(key_) + 1.0
        KV = jnp.einsum('nsh,nsh->nh', K, value, precision='highest')
        Ksum = jnp.sum(K, axis=1)
        Z = 1.0 / (Q * Ksum[:, None, :] + 1e-06)
        V = Q * KV[:, None, :] * Z
        out = V @ wo + bo
        return jax.nn.gelu(out, approximate=True)

    def _L0_ffn_ref(x, Wr, br, W1, b1, W2, b2):
        import jax, jax.numpy as jnp
        import numpy as np
        B, S, D, E, H = (2, 128, 128, 16, 256)
        TOP_K = 2
        TEMP = 1.0
        token_shape = x.shape[:-1]
        d = x.shape[-1]
        xt = x.reshape(-1, d)
        T = xt.shape[0]
        logits = (xt @ Wr + br) / TEMP
        probs = jax.nn.softmax(logits, axis=-1)
        w, idx = jax.lax.top_k(probs, TOP_K)
        w = w / jnp.clip(jnp.sum(w, axis=-1, keepdims=True), 1e-09)
        comb = jnp.zeros((T, E), dtype=xt.dtype)
        comb = comb.at[jnp.arange(T)[:, None], idx].add(w)
        h = jax.nn.gelu(jnp.einsum('td,edh->teh', xt, W1) + b1, approximate=False)
        o = jnp.einsum('teh,eho->teo', h, W2) + b2
        y = jnp.einsum('teo,te->to', o, comb)
        y = xt + y
        return y.reshape(*token_shape, d)

    def _L1_attn_ref(x, Wq, Wk, Wv, Wo):
        import jax, jax.numpy as jnp
        import numpy as np
        NUM_HEADS = 16
        HIDDEN = 128
        HEAD_DIM = HIDDEN // NUM_HEADS
        B, L = (2, 256)
        b, l, _ = x.shape
        q = (x @ Wq.T).reshape(b, l, NUM_HEADS, HEAD_DIM)
        k = (x @ Wk.T).reshape(b, l, NUM_HEADS, HEAD_DIM)
        v = (x @ Wv.T).reshape(b, l, NUM_HEADS, HEAD_DIM)
        q = jax.nn.elu(q) + 1.0
        k = jax.nn.elu(k) + 1.0
        kv = jnp.einsum('blhd,blhe->blhde', k, v)
        kv_cumsum = jnp.cumsum(kv, axis=1)
        k_cumsum = jnp.cumsum(k, axis=1)
        out = jnp.einsum('blhd,blhde->blhe', q, kv_cumsum)
        normalizer = jnp.clip(jnp.einsum('blhd,blhd->blh', q, k_cumsum), 1e-06, None)
        out = out / normalizer[..., None]
        out = out.reshape(b, l, HIDDEN)
        return out @ Wo.T

    def _L1_ffn_ref(tokens, gate_w, expert_w, expert_b):
        import jax, jax.numpy as jnp
        import numpy as np
        B, S, H, E = (2, 256, 128, 16)
        b, s, h = tokens.shape
        logits = jnp.einsum('bsh,eh->bse', tokens, gate_w)
        weights = jax.nn.softmax(logits, axis=-1)
        top2_w, top2_idx = jax.lax.top_k(weights, 2)
        flat = tokens.reshape(b * s, h)
        flat_w = top2_w.reshape(b * s, 2)
        flat_idx = top2_idx.reshape(b * s, 2)
        y = jax.nn.relu(jnp.einsum('nh,edh->ned', flat, expert_w) + expert_b[None, :, :])
        sel = jnp.take_along_axis(y, flat_idx[:, :, None], axis=1)
        out = jnp.sum(sel * flat_w[:, :, None], axis=1)
        return out.reshape(b, s, h)
    x = L0_attn_x
    x = x + 0.5 * _L0_ffn_ref(_layernorm(x, axis=-1), L0_ffn_Wr, L0_ffn_br, L0_ffn_W1, L0_ffn_b1, L0_ffn_W2, L0_ffn_b2)
    x = x + _L0_attn_ref(_layernorm(x, axis=-1), L0_attn_wq, L0_attn_bq, L0_attn_wk, L0_attn_bk, L0_attn_wv, L0_attn_bv, L0_attn_wo, L0_attn_bo)
    x = x + 0.5 * _L0_ffn_ref(_layernorm(x, axis=-1), L0_ffn_Wr, L0_ffn_br, L0_ffn_W1, L0_ffn_b1, L0_ffn_W2, L0_ffn_b2)
    x = x + 0.5 * _L1_ffn_ref(_layernorm(x, axis=-1), L1_ffn_gate_w, L1_ffn_expert_w, L1_ffn_expert_b)
    x = x + _L1_attn_ref(_layernorm(x, axis=-1), L1_attn_Wq, L1_attn_Wk, L1_attn_Wv, L1_attn_Wo)
    x = x + 0.5 * _L1_ffn_ref(_layernorm(x, axis=-1), L1_ffn_gate_w, L1_ffn_expert_w, L1_ffn_expert_b)
    return x

_drawn_inputs = setup_inputs


def setup_inputs(seed=0):
    import zlib

    import numpy as np

    out = dict(_drawn_inputs(seed))
    spreads = {'L0_attn_bq': (0.0, 2.0),
     'L0_attn_bk': (0.0, 2.0),
     'L0_attn_bv': (0.0, 0.1),
     'L0_attn_bo': (0.0, 0.1),
     'L0_ffn_br': (0.0, 0.1),
     'L0_ffn_b1': (0.0, 0.1),
     'L0_ffn_b2': (0.0, 0.1)}
    factors = {'L0_attn_wq': 49.17, 'L1_attn_Wq': 4.56, 'L1_ffn_expert_b': 53.211}
    for name, (base, spread) in spreads.items():
        noise = np.random.default_rng([zlib.crc32(name.encode()), seed]).standard_normal(out[name].shape)
        drawn = base * np.exp(spread * noise) if base else spread * noise
        out[name] = jnp.asarray(drawn.astype(out[name].dtype))
    for name, factor in factors.items():
        out[name] = (out[name] * factor).astype(out[name].dtype)
    return out
```

```python
import concourse.bass as bass
from concourse import mybir
from contextlib import ExitStack



def build_program(nc, x, wq, bq, wk, bk, wv, bv, wo, bo, Wr, br, W1, b1, W2, b2,
                  Wq, Wk, Wv, Wo, gate_w, expert_w, expert_b, out):
    f32 = mybir.dt.float32
    f32r = mybir.dt.float32r
    ALU = mybir.AluOpType
    ACT = mybir.ActivationFunctionType
    AX = mybir.AxisListType.X

    P = 128
    B, S, D = x.shape
    E, _, H = W1.shape
    TOK = B * S
    CH = 512
    NCH = TOK // CH
    TPC = CH // P
    HC = H // P
    NSEQ = CH // S
    TPS = S // P
    HEADS, HD = 16, 8
    LN_EPS = 1e-5
    RING_HW = 3
    HALF = E // 2
    GQ = 4
    WROUNDS = 6
    MOE0_A, ATT0, MOE0_B, MOE1_A, ATT1, MOE1_B = range(6)
    SLOTS = 2 * NCH * E
    LAG = 2

    comb_dram = nc.dram_tensor("comb_rows", [2, E, TOK], f32, kind="Internal").ap()

    with ExitStack() as ctx:
        def sb(name, shape, dt=f32):
            return ctx.enter_context(nc.sbuf_tensor(name, shape, dt))

        def sem(name):
            return ctx.enter_context(nc.semaphore(name))

        ident = sb("ident", [P, P])
        tri = sb("tri", [P, P])
        ones = sb("ones", [P, P])
        ones2 = sb("ones2", [2, P], f32r)
        rev = sb("rev", [P, E])
        mhalf = sb("mhalf", [P, TPC])
        w1h, w1l = sb("w1h", [P, E * H], f32r), sb("w1l", [P, E * H], f32r)
        w2s = sb("w2s", [P, E * HC * D])
        b1row = sb("b1row", [E * HC, P])
        b1col = sb("b1col", [P, E * HC])
        b2s = sb("b2s", [E, D])
        brc = sb("brc", [E, 1])
        wrh, wrl = sb("wrh", [P, P], f32r), sb("wrl", [P, P], f32r)
        gth, gtl = sb("gth", [P, P], f32r), sb("gtl", [P, P], f32r)
        qkv0h, qkv0l = sb("qkv0h", [P, 3 * P], f32r), sb("qkv0l", [P, 3 * P], f32r)
        bqkv = sb("bqkv", [P, 3])
        wos = sb("wos", [P, D])
        bos = sb("bos", [1, D])
        qkv1h, qkv1l = sb("qkv1h", [P, 3 * P], f32r), sb("qkv1l", [P, 3 * P], f32r)
        woT = sb("woT", [P, P])
        weh, wel = sb("weh", [P, E * D], f32r), sb("wel", [P, E * D], f32r)
        ber = sb("ber", [2, E * D], f32r)
        stage = sb("stage", [P, E * H])
        stage2 = sb("stage2", [P, 2 * P + 3 * P + 2 * P])
        X = sb("X", [P, NCH * TPC * D])
        stats = sb("stats", [P, TPC, 6])
        mv = sb("mv", [P, TPC, 2])
        rstd = sb("rstd", [P, TPC])
        vare = sb("vare", [P, TPC])
        xn = sb("xn", [P, TPC * D])
        xnh = sb("xnh", [P, TPC * D])
        xbh, xbl = sb("xbh", [P, TOK], f32r), sb("xbl", [P, TOK], f32r)
        xsh, xsl = sb("xsh", [P, CH], f32r), sb("xsl", [P, CH], f32r)
        lgT = sb("lgT", [E, CH])
        sm = [sb(f"sm{i}", [P, TPC, E]) for i in range(9)]
        sc = [sb(f"sc{i}", [P, TPC]) for i in range(8)]
        comb = sb("comb", [P, TPC, E])
        combT = sb("combT", [E, TOK])
        bc = sb("bc", [P, 2, GQ, CH])
        g = sb("g", [P, 2, HC, CH])
        hw = sb("hw", [P, RING_HW, HC, CH])
        ysb = sb("ysb", [P, CH])
        t_r = stage[:, 0:2 * CH].rearrange("p (a n) -> p a n", a=2)
        t_m = stage[:, 2 * CH:4 * CH].rearrange("p (a n) -> p a n", a=2)
        rel = stage[:, 0:E * D]
        kvo = stage[:, E * D:2 * E * D].rearrange("p (a n) -> p a n", a=TPS)
        be_raw = stage[0:2, E * D:2 * E * D]
        side1 = sb("side1", [P, 2 * CH])
        vv, osb = side1[:, 0:CH], side1[:, CH:2 * CH]
        prod = side1[:, :]
        kvs = sb("kvs", [P, 2, NSEQ])
        red = sb("red", [P, D])
        qk_r = sb("qk_r", [P, 2 * P])
        qk_m = sb("qk_m", [P, 2 * P])
        qk = sb("qk", [P, TPS, 2 * P])
        v1 = sb("v1", [P, P])
        prn = sb("prn", [P, P])
        nrm = sb("nrm", [P, HEADS])
        att = sb("att", [P, P])
        attT = sb("attT", [P, P])

        ph = ctx.enter_context(nc.psum_tensor("ph", [P, 2, HC, CH], f32))
        py = ctx.enter_context(nc.psum_tensor("py", [P, CH], f32))
        ps = ctx.enter_context(nc.psum_tensor("ps", [P, 3, CH], f32))

        x_in = [sem(f"x_in{c}") for c in range(NCH)]
        w_in = {n: sem("in_" + n) for n in ("w1", "w2", "small", "l1", "we", "be")}
        const_ready = sem("const_ready")
        prep_t = sem("prep_transposed")
        prep_v = sem("prep_split")
        b1_ps, b1_ready = sem("b1_ps"), sem("b1_ready")
        wt_ps, wt_done, be_done = sem("wt_ps"), sem("wt_done"), sem("be_done")
        dve_step = sem("dve_step")
        pool_step = sem("pool_step")
        act_step = sem("act_step")
        h_ready = sem("h_ready")
        g_ready = sem("g_ready")
        hw_ready = sem("hw_ready")
        slot_done = sem("slot_done")
        y_ready = sem("y_ready")
        y_out = sem("y_out")
        comb_row = sem("comb_row")
        bc_in = [sem("bc_in0"), sem("bc_in1")]
        names = ("stat", "rstd", "xn", "xt_ps", "xh", "xl", "res", "lgt_ps", "lgt", "lg_ps", "shift", "expd",
                 "comb", "ct_ps", "ct", "yt_ps")
        SG = {n: sem(n) for n in names}
        a0 = {n: sem("a0_" + n) for n in ("q_ps", "k_ps", "v_ps", "relq", "relk", "v", "minq", "mink", "expq", "expk",
                                          "vz", "o_ps", "o")}
        f1 = {l: {n: sem(f"f{l}_{n}") for n in ("y_ps", "relu", "red")} for l in (MOE1_A, MOE1_B)}
        a1 = {n: sem("a1_" + n) for n in ("qkv_ps", "relu", "v", "min", "exp", "kv", "cum_ps", "att", "at_ps", "at",
                                          "o_ps", "x")}
        stored = sem("stored")

        x_t = x.rearrange("b (a p) d -> p (b a) d", p=P)
        out_t = out.rearrange("b (a p) d -> p (b a) d", p=P)

        block = ctx.enter_context(nc.Block())

        def col(c):
            return slice(c * CH, (c + 1) * CH)

        def drive(main, side):
            for _ in side(-1):
                pass
            done = 0
            for k in range(2 * NCH + 1):
                end = min(E * (k + 1) + LAG, SLOTS + LAG)
                steps = list(range(STEPS[k]))
                gen = side(k)
                start = done
                for i in steps:
                    upto = start + ((end - start) * (i + 1)) // (len(steps) + 1)
                    while done < upto:
                        main(done)
                        done += 1
                    next(gen)
                while done < end:
                    main(done)
                    done += 1
                assert next(gen, "end") == "end"

        N_LN, N_RT, N_CT, N_C0, N_A0, N_F1, N_A1 = 3, 3, 1, 1, 3, TPC, 3 * TPS * NSEQ

        def plan(k):
            todo = [("be", MOE1_A, 0)] if k == 1 else []
            if k == -1:
                return [("ln", MOE0_A, 0), ("rt", MOE0_A, 0), ("ct", MOE0_A, 0)]
            if 1 <= k <= NCH:
                c = k - 1
                todo += [("c0", MOE0_A, c), ("ln", ATT0, c), ("a0", ATT0, c),
                         ("ln", MOE0_B, c), ("rt", MOE0_B, c), ("ct", MOE0_B, c)]
            if k + 1 < NCH:
                todo += [("ln", MOE0_A, k + 1), ("rt", MOE0_A, k + 1), ("ct", MOE0_A, k + 1)]
            if k == 0:
                todo += [("wt", MOE1_A, 0)]
            if k > NCH:
                c = k - 1 - NCH
                todo += [("c0", MOE0_B, c), ("ln", MOE1_A, c), ("rt", MOE1_A, c), ("f1", MOE1_A, c),
                         ("ln", ATT1, c), ("a1", ATT1, c),
                         ("ln", MOE1_B, c), ("rt", MOE1_B, c), ("f1", MOE1_B, c)]
            return todo

        STAGE_OF = {"lgt_ps": "rt", "lgt": "rt", "lg_ps": "rt", "shift": "rt", "expd": "rt", "comb": "rt",
                    "ct_ps": "ct", "ct": "ct", "yt_ps": "c0"}
        ORDER = [t for k in range(-1, 2 * NCH + 1) for t in plan(k)]

        def nth_side(signal, l, c):
            stage_ = STAGE_OF.get(signal, "ln")
            same = [t for t in ORDER if t[0] == stage_ and (signal != "res" or moe0(t[1]))]
            return same.index((stage_, l, c)) + 1

        COUNT = {"ln": N_LN, "rt": N_RT, "ct": N_CT, "c0": N_C0, "a0": N_A0, "f1": N_F1, "a1": N_A1, "wt": WROUNDS, "be": 1}
        STEPS = {k: sum(COUNT[s] for s, _, _ in plan(k)) for k in range(2 * NCH + 1)}

        def sides(table):
            def side(k):
                for s, l, c in plan(k):
                    n = 0
                    for _ in table[s](l, c):
                        n += 1
                        yield
                    assert n == COUNT[s], (s, n)
            return side

        def split_dst(l, c):
            return (xbh[:, col(c)], xbl[:, col(c)]) if l in (MOE0_A, MOE0_B) else (xsh[:, :], xsl[:, :])

        def moe0(l):
            return l in (MOE0_A, MOE0_B)

        def nth(l, c):
            return (0 if l == MOE0_A else NCH) + c

        @block.sync
        def _(sp):
            for c in range(1):
                sp.dma_start(X[:, col(c)].rearrange("p (t d) -> p t d", d=D), x_t[:, TPC * c:TPC * (c + 1), :]).then_inc(x_in[c], 16)
            sp.dma_start(stage2[:, 0:E], Wr).then_inc(w_in["small"], 16)
            sp.dma_start(brc[:, :], br.rearrange("(e a) -> e a", a=1)).then_inc(w_in["small"], 16)
            sp.dma_start(b1row[:, :], b1.rearrange("e (c p) -> (e c) p", p=P)).then_inc(w_in["small"], 16)
            sp.dma_start(stage[:, :].rearrange("p (e h) -> p e h", e=E), W1.rearrange("e d h -> d e h")).then_inc(w_in["w1"], 16)
            sp.dma_start(w2s[:, :].rearrange("p (e c o) -> p e c o", e=E, c=HC), W2.rearrange("e (c p) o -> p e c o", p=P)).then_inc(w_in["w2"], 16)
            sp.dma_start(b2s[:, :], b2).then_inc(w_in["w2"], 16)
            for i, (w, b) in enumerate(((wq, bq), (wk, bk), (wv, bv))):
                sp.dma_start(stage2[:, P * (2 + i):P * (3 + i)], w).then_inc(w_in["small"], 16)
                sp.dma_start(bqkv[:, i:i + 1], b.rearrange("(p a) -> p a", a=1)).then_inc(w_in["small"], 16)
            sp.dma_start(wos[:, :], wo).then_inc(w_in["small"], 16)
            sp.dma_start(bos[:, :], bo.rearrange("(a p) -> a p", a=1)).then_inc(w_in["small"], 16)
            for c in range(1, NCH):
                sp.dma_start(X[:, col(c)].rearrange("p (t d) -> p t d", d=D), x_t[:, TPC * c:TPC * (c + 1), :]).then_inc(x_in[c], 16)
            def second_weights():
                sp.wait_ge(prep_v, 4)
                sp.dma_start(stage[:, 0:E * D].rearrange("p (e h) -> p e h", e=E), expert_w.rearrange("e d h -> d e h")).then_inc(w_in["we"], 16)
                for i, w in enumerate((Wq, Wk, Wv, Wo)):
                    sp.dma_start(stage[:, E * D + P * i:E * D + P * (i + 1)], w).then_inc(w_in["l1"], 16)
                sp.dma_start(stage[0:E, E * D + 4 * P:E * D + 5 * P], gate_w).then_inc(w_in["l1"], 16)

            for n in range(2 * NCH):
                l, c = n // NCH, n % NCH
                sp.wait_ge(SG["ct"], nth_side("ct", (MOE0_A, MOE0_B)[l], c))
                sp.dma_start(comb_dram[l, :, col(c)], combT[:, col(c)]).then_inc(comb_row, 16)
                sp.wait_ge(comb_row, 16 * (n + 1))
                for q in range(E // GQ):
                    k = n * (E // GQ) + q
                    if k >= 2:
                        sp.wait_ge(hw_ready, GQ * (k - 1))
                    sp.dma_start(bc[:, k % 2, :, :], comb_dram[l, q * GQ:(q + 1) * GQ, col(c)].partition_broadcast(P)).then_inc(bc_in[k % 2], 16)
                    if k == 1:
                        second_weights()
                if n == 0:
                    sp.wait_ge(wt_done, WROUNDS)
                    for r in range(2):
                        sp.dma_start(be_raw[r:r + 1, :], expert_b.rearrange("(a e) d -> a (e d)", a=1)).then_inc(w_in["be"], 16)
            for c in range(NCH):
                sp.wait_ge(f1[MOE1_B]["red"], TPC * (c + 1))
                sp.dma_start(out_t[:, TPC * c:TPC * (c + 1), :], X[:, col(c)].rearrange("p (t d) -> p t d", d=D)).then_inc(stored, 16)
            sp.wait_ge(stored, 16 * NCH)

        @block.gpsimd
        def _(pool):
            nc.gpsimd.memset(ident[:, :], 0.0).then_inc(pool_step, 1)
            nc.gpsimd.memset(tri[:, :], 1.0).then_inc(pool_step, 1)
            nc.gpsimd.memset(ones[:, :], 1.0)
            nc.gpsimd.memset(mhalf[:, :], -0.5)
            nc.gpsimd.iota(rev[:, :], pattern=[[-1, E]], base=E, channel_multiplier=0,
                           allow_small_or_imprecise_dtypes=True)
            pool.wait_ge(pool_step, 2)
            nc.gpsimd.affine_select(out=ident[:, :], in_=ident[:, :], compare_op=ALU.not_equal, fill=1.0, base=0,
                                    pattern=[[-1, P]], channel_multiplier=1)
            nc.gpsimd.affine_select(out=tri[:, :], in_=tri[:, :], compare_op=ALU.is_ge, fill=0.0, base=0,
                                    pattern=[[1, P]], channel_multiplier=-1).then_inc(const_ready, 1)
            steps = [2]
            last = []

            def ln(l, c):
                pool.wait_ge(SG["stat"], nth_side("stat", l, c))
                nc.gpsimd.tensor_scalar(vare[:, :], mv[:, :, 1], LN_EPS, None, ALU.add).then_inc(pool_step, 1)
                steps[0] += 1
                pool.wait_ge(pool_step, steps[0])
                nc.gpsimd.tensor_tensor(rstd[:, :], vare[:, :], mhalf[:, :], ALU.pow).then_inc(SG["rstd"], 1)
                if moe0(l):
                    pool.wait_ge(SG["xn"], nth_side("xn", l, c))
                    if last:
                        pool.wait_ge(*last.pop())
                    nc.gpsimd.tensor_scalar(xnh[:, :], xn[:, :], 0.5, 1.0, ALU.mult, ALU.mult).then_inc(pool_step, 1)
                    steps[0] += 1
                    pool.wait_ge(pool_step, steps[0])
                    nc.gpsimd.tensor_tensor(X[:, col(c)], X[:, col(c)], xnh[:, :], ALU.add).then_inc(SG["res"], 1)
                    last.append((SG["res"], nth_side("res", l, c)))
                for _ in range(N_LN):
                    yield

            def nothing(n):
                def gen(l, c):
                    for _ in range(n):
                        yield
                return gen

            drive(lambda s: None, sides({"ln": ln, "rt": nothing(N_RT), "ct": nothing(N_CT), "c0": nothing(N_C0),
                                         "a0": nothing(N_A0), "f1": nothing(N_F1), "a1": nothing(N_A1), "wt": nothing(WROUNDS), "be": nothing(1)}))

        @block.scalar
        def _(act):
            act.wait_ge(w_in["w1"], 16)
            nc.scalar.activation(w1h[:, 0:E * H // 2], stage[:, 0:E * H // 2], ACT.Copy).then_inc(prep_t, 1)
            nc.scalar.activation(w1h[:, E * H // 2:], stage[:, E * H // 2:], ACT.Copy).then_inc(prep_t, 1)

            def ln(l, c):
                yield
                yield
                act.wait_ge(SG["xt_ps"], nth_side("xt_ps", l, c))
                nc.scalar.activation(split_dst(l, c)[0], ps[:, 0, :], ACT.Copy).then_inc(SG["xh"], 1)
                yield

            def rt(l, c):
                act.wait_ge(SG["lgt_ps"], nth_side("lgt_ps", l, c))
                if moe0(l):
                    nc.scalar.activation(lgT[:, :], ps[0:E, 1, :], ACT.Identity, bias=brc[:, :]).then_inc(SG["lgt"], 1)
                else:
                    nc.scalar.activation(lgT[:, :], ps[0:E, 1, :], ACT.Copy).then_inc(SG["lgt"], 1)
                yield
                act.wait_ge(SG["shift"], nth_side("shift", l, c))
                nc.scalar.activation(sm[1][:, :, :], sm[0][:, :, :], ACT.Exp).then_inc(SG["expd"], 1)
                yield
                yield

            def ct(l, c):
                act.wait_ge(SG["ct_ps"], nth_side("ct_ps", l, c))
                nc.scalar.activation(combT[:, col(c)], ps[0:E, 1, :], ACT.Copy).then_inc(SG["ct"], 1)
                yield

            def c0(l, c):
                yield

            def wt(l, c):
                for _ in range(WROUNDS):
                    yield

            def be(l, c):
                yield

            def a0_(l, c):
                for i, (src, dst) in enumerate((("q_ps", "relq"), ("k_ps", "relk"))):
                    act.wait_ge(a0[src], c + 1)
                    nc.scalar.activation(t_r[:, i, :], ps[:, 1 + i, :], ACT.Relu, bias=bqkv[:, i:i + 1]).then_inc(a0[dst], 1)
                act.wait_ge(a0["v_ps"], c + 1)
                nc.scalar.activation(vv, ps[:, 0, :], ACT.Identity, bias=bqkv[:, 2:3]).then_inc(a0["v"], 1)
                yield
                for i, n in enumerate(("q", "k")):
                    act.wait_ge(a0["min" + n], c + 1)
                    nc.scalar.activation(t_m[:, i, :], t_m[:, i, :], ACT.Exp).then_inc(a0["exp" + n], 1)
                yield
                act.wait_ge(a0["o_ps"], c + 1)
                nc.scalar.activation(osb, ps[:, 1, :], ACT.Gelu_apprx_tanh).then_inc(a0["o"], 1)
                yield

            def f1_(l, c):
                for j in range(TPC):
                    for q in range(E // 4):
                        u = c * TPC * 4 + 4 * j + q
                        act.wait_ge(f1[l]["y_ps"], u + 1)
                        if j and q == 0:
                            act.wait_ge(f1[l]["red"], c * TPC + j)
                        for i in range(4):
                            e = 4 * q + i
                            ins = nc.scalar.activation(rel[:, e * D:(e + 1) * D], ps[:, u % 3, i * D:(i + 1) * D], ACT.Relu,
                                                       scale=comb[:, j, e:e + 1])
                        ins.then_inc(f1[l]["relu"], 1)
                    yield

            def a1_(l, c):
                for s in range(NSEQ):
                    for j in range(TPS):
                        u = (c * NSEQ + s) * TPS + j
                        act.wait_ge(a1["qkv_ps"], u + 1)
                        if u:
                            act.wait_ge(a1["kv"], u)
                        nc.scalar.activation(qk_r[:, :], ps[:, 1, 0:2 * P], ACT.Relu).then_inc(a1["relu"], 1)
                        nc.scalar.activation(v1[:, :], ps[:, 1, 2 * P:3 * P], ACT.Copy).then_inc(a1["v"], 1)
                        act.wait_ge(a1["min"], u + 1)
                        nc.scalar.activation(qk_m[:, :], qk_m[:, :], ACT.Exp).then_inc(a1["exp"], 1)
                        yield
                    for j in range(TPS):
                        u = (c * NSEQ + s) * TPS + j
                        yield
                        act.wait_ge(a1["at_ps"], u + 1)
                        nc.scalar.activation(attT[:, :], ps[:, 2, 0:P], ACT.Copy).then_inc(a1["at"], 1)
                        yield

            def main(s):
                n, e = divmod(s, E)
                if s == 0:
                    act.wait_ge(b1_ready, 1)
                if s < SLOTS:
                    for h in range(HC):
                        act.wait_ge(h_ready, HC * s + h + 1)
                        if s >= 2:
                            act.wait_ge(hw_ready, s - 1)
                        nc.scalar.activation(g[:, s % 2, h, :], ph[:, s % 2, h, :], ACT.Gelu,
                                             bias=b1col[:, HC * e + h:HC * e + h + 1]).then_inc(g_ready, 1)
                if e == LAG - 1 and n:
                    act.wait_ge(y_ready, n)
                    if n >= 2:
                        act.wait_ge(SG["yt_ps"], n - 1)
                    nc.scalar.activation(ysb[:, :], py[:, :], ACT.Copy).then_inc(y_out, 1)

            drive(main, sides({"ln": ln, "rt": rt, "ct": ct, "c0": c0, "a0": a0_, "f1": f1_, "a1": a1_, "wt": wt, "be": be}))

        @block.vector
        def _(dve):
            count = [0]

            def link(ins):
                count[0] += 1
                ins.then_inc(dve_step, 1)
                dve.wait_ge(dve_step, count[0])

            V = nc.vector
            dve.wait_ge(w_in["small"], 16 * 11)
            for t in (gth, gtl, wrh, wrl):
                ins = V.memset(t[:, :].bitcast(f32), 0.0)
            link(ins)
            link(V.tensor_copy(wrh[:, 0:E], stage2[:, 0:E]))
            V.tensor_tensor(wrl[:, 0:E], stage2[:, 0:E], wrh[:, 0:E].bitcast(f32), ALU.subtract)
            link(V.tensor_copy(qkv0h[:, :], stage2[:, 2 * P:5 * P]))
            V.tensor_tensor(qkv0l[:, :], stage2[:, 2 * P:5 * P], qkv0h[:, :].bitcast(f32), ALU.subtract).then_inc(prep_v, 1)
            dve.wait_ge(const_ready, 1)
            V.tensor_copy(ones2[:, :], ones[0:2, :]).then_inc(prep_v, 1)
            dve.wait_ge(b1_ps, 1)
            V.tensor_copy(b1col[:, :], py[:, 0:E * HC]).then_inc(b1_ready, 1)
            for i in range(2):
                dve.wait_ge(prep_t, i + 1)
                half = slice(i * E * H // 2, (i + 1) * E * H // 2)
                V.tensor_tensor(w1l[:, half], stage[:, half], w1h[:, half].bitcast(f32), ALU.subtract).then_inc(prep_v, 1)

            def ln(l, c):
                if l == MOE0_A:
                    dve.wait_ge(x_in[c], 16)
                for j in range(TPC):
                    ins = V.bn_stats(stats[:, j, :], X[:, c * CH + j * D:c * CH + (j + 1) * D])
                link(ins)
                for j in range(TPC):
                    ins = V.bn_aggr(mv[:, j, :], stats[:, j, :])
                ins.then_inc(SG["stat"], 1)
                yield
                dve.wait_ge(SG["rstd"], nth_side("rstd", l, c))
                for j in range(TPC):
                    ins = V.tensor_scalar(xn[:, j * D:(j + 1) * D], X[:, c * CH + j * D:c * CH + (j + 1) * D],
                                          mv[:, j, 0:1], rstd[:, j:j + 1], ALU.subtract, ALU.mult)
                ins.then_inc(SG["xn"], 1)
                yield
                dve.wait_ge(SG["xh"], nth_side("xh", l, c))
                hi, lo = split_dst(l, c)
                V.tensor_tensor(lo, ps[:, 0, :], hi.bitcast(f32), ALU.subtract).then_inc(SG["xl"], 1)
                yield

            def bcast(t):
                return t[:, :].unsqueeze(2).to_broadcast([P, TPC, E])

            def rt(l, c):
                yield
                lg = ps[:, 2, 0:TPC * E].rearrange("p (t e) -> p t e", e=E)
                dve.wait_ge(SG["lg_ps"], nth_side("lg_ps", l, c))
                link(V.tensor_reduce(sc[0][:, :], lg, AX, ALU.max))
                V.tensor_tensor(sm[0][:, :, :], lg, bcast(sc[0]), ALU.subtract).then_inc(SG["shift"], 1)
                yield
                dve.wait_ge(SG["expd"], nth_side("expd", l, c))
                link(V.tensor_reduce(sc[1][:, :], sm[1][:, :, :], AX, ALU.add))
                link(V.reciprocal(sc[2][:, :], sc[1][:, :]))
                p = sm[2][:, :, :]
                link(V.tensor_tensor(p, sm[1][:, :, :], bcast(sc[2]), ALU.mult))
                revb = rev[:, :].unsqueeze(1).to_broadcast([P, TPC, E])
                link(V.tensor_reduce(sc[3][:, :], p, AX, ALU.max))
                link(V.tensor_tensor(sm[3][:, :, :], p, bcast(sc[3]), ALU.is_equal))
                link(V.tensor_tensor(sm[4][:, :, :], sm[3][:, :, :], revb, ALU.mult))
                link(V.tensor_reduce(sc[4][:, :], sm[4][:, :, :], AX, ALU.max))
                link(V.tensor_tensor(sm[5][:, :, :], sm[4][:, :, :], bcast(sc[4]), ALU.is_equal))
                link(V.scalar_tensor_tensor(sm[6][:, :, :], sm[5][:, :, :], -2.0, p, ALU.mult, ALU.add))
                link(V.tensor_reduce(sc[5][:, :], sm[6][:, :, :], AX, ALU.max))
                link(V.tensor_tensor(sm[3][:, :, :], sm[6][:, :, :], bcast(sc[5]), ALU.is_equal))
                link(V.tensor_tensor(sm[4][:, :, :], sm[3][:, :, :], revb, ALU.mult))
                link(V.tensor_reduce(sc[6][:, :], sm[4][:, :, :], AX, ALU.max))
                link(V.tensor_tensor(sm[7][:, :, :], sm[4][:, :, :], bcast(sc[6]), ALU.is_equal))
                link(V.tensor_tensor(sm[8][:, :, :], sm[5][:, :, :], sm[7][:, :, :], ALU.add))
                if moe0(l):
                    link(V.tensor_tensor(sm[3][:, :, :], sm[8][:, :, :], p, ALU.mult))
                    link(V.tensor_tensor(sc[7][:, :], sc[3][:, :], sc[5][:, :], ALU.add))
                    link(V.tensor_scalar(sc[6][:, :], sc[7][:, :], 1e-9, None, ALU.max))
                    link(V.reciprocal(sc[4][:, :], sc[6][:, :]))
                    V.tensor_tensor(comb[:, :, :], sm[3][:, :, :], bcast(sc[4]), ALU.mult).then_inc(SG["comb"], 1)
                else:
                    V.tensor_tensor(comb[:, :, :], sm[8][:, :, :], p, ALU.mult).then_inc(SG["comb"], 1)
                yield

            def ct(l, c):
                yield

            def c0(l, c):
                dve.wait_ge(SG["yt_ps"], nth_side("yt_ps", l, c))
                dve.wait_ge(SG["res"], nth_side("res", l, c))
                link(V.scalar_tensor_tensor(X[:, col(c)], ps[:, 0, :], 0.5, X[:, col(c)], ALU.mult, ALU.add))
                yield

            def a0_(l, c):
                for i, n in enumerate(("q", "k")):
                    dve.wait_ge(a0["rel" + n], c + 1)
                    V.tensor_scalar(t_m[:, i, :], ps[:, 1 + i, :], bqkv[:, i:i + 1], 0.0, ALU.add, ALU.min).then_inc(a0["min" + n], 1)
                yield
                dve.wait_ge(a0["expk"], c + 1)
                link(V.scalar_tensor_tensor(t_r[:, :, :], t_m[:, :, :], -1.0, t_r[:, :, :], ALU.add, ALU.add))
                dve.wait_ge(a0["v"], c + 1)
                for s in range(NSEQ):
                    q = slice(s * S, (s + 1) * S)
                    V.tensor_scalar(t_m[:, 1, q], t_r[:, 1, q], 1.0, None, ALU.add, ALU.add, accum_out=kvs[:, 0, s:s + 1])
                    V.scalar_tensor_tensor(osb[:, q], t_r[:, 1, q], 1.0, vv[:, q], ALU.add, ALU.mult,
                                           accum_out=kvs[:, 1, s:s + 1])
                link(V.tensor_scalar(t_m[:, 0, :], t_r[:, 0, :], 1.0, None, ALU.add))
                for s in range(NSEQ):
                    q = slice(s * S, (s + 1) * S)
                    ins = V.tensor_scalar(t_r[:, 1, q], t_m[:, 0, q], kvs[:, 0, s:s + 1], 1e-6, ALU.mult, ALU.add)
                link(ins)
                link(V.reciprocal(t_r[:, 0, :], t_r[:, 1, :]))
                for s in range(NSEQ):
                    q = slice(s * S, (s + 1) * S)
                    ins = V.scalar_tensor_tensor(vv[:, q], t_m[:, 0, q], kvs[:, 1, s:s + 1], t_r[:, 0, q], ALU.mult, ALU.mult)
                ins.then_inc(a0["vz"], 1)
                yield
                dve.wait_ge(a0["o"], c + 1)
                link(V.tensor_tensor(X[:, col(c)], X[:, col(c)], osb, ALU.add))
                yield

            def f1_(l, c):
                for j in range(TPC):
                    dve.wait_ge(f1[l]["relu"], c * TPC * 4 + 4 * (j + 1))
                    link(V.tensor_reduce(red[:, :], rel.rearrange("p (e d) -> p d e", e=E), AX, ALU.add))
                    xs_ = X[:, c * CH + j * D:c * CH + (j + 1) * D]
                    ins = V.scalar_tensor_tensor(xs_, red[:, :], 0.5, xs_, ALU.mult, ALU.add)
                    ins.then_inc(f1[l]["red"], 1)
                    dve.wait_ge(f1[l]["red"], c * TPC + j + 1)
                    yield

            def a1_(l, c):
                for s in range(NSEQ):
                    for j in range(TPS):
                        u = (c * NSEQ + s) * TPS + j
                        dve.wait_ge(a1["v"], u + 1)
                        V.tensor_scalar(qk_m[:, :], ps[:, 1, 0:2 * P], 0.0, None, ALU.min).then_inc(a1["min"], 1)
                        dve.wait_ge(a1["exp"], u + 1)
                        link(V.scalar_tensor_tensor(qk_r[:, :], qk_m[:, :], -1.0, qk_r[:, :], ALU.add, ALU.add))
                        link(V.tensor_scalar(qk[:, j, :], qk_r[:, :], 1.0, None, ALU.add))
                        kb = qk[:, j, P:2 * P].rearrange("p (h d) -> p h d", d=HD).unsqueeze(3).to_broadcast([P, HEADS, HD, HD])
                        vb = v1[:, :].rearrange("p (h e) -> p h e", e=HD).unsqueeze(2).to_broadcast([P, HEADS, HD, HD])
                        V.tensor_tensor(kvo[:, j, :].rearrange("p (h d e) -> p h d e", d=HD, e=HD), kb, vb, ALU.mult).then_inc(a1["kv"], 1)
                        yield
                    for j in range(TPS):
                        u = (c * NSEQ + s) * TPS + j
                        dve.wait_ge(a1["cum_ps"], u + 1)
                        qb = qk[:, j, 0:P].unsqueeze(2).to_broadcast([P, P, HD])
                        link(V.tensor_tensor(prod.rearrange("p (k e) -> p k e", e=HD), qb,
                                        ps[:, 0:2, :].rearrange("p b (k e) -> p (b k) e", e=HD), ALU.mult))
                        link(V.tensor_tensor(prn[:, :], qk[:, j, 0:P], ps[:, 2, 0:P], ALU.mult))
                        V.tensor_reduce(att[:, :].rearrange("p (h e) -> p h e", e=HD),
                                        prod.rearrange("p (h d e) -> p h e d", d=HD, e=HD), AX, ALU.add)
                        link(V.tensor_reduce(nrm[:, :], prn[:, :].rearrange("p (h d) -> p h d", d=HD), AX, ALU.add))
                        link(V.tensor_scalar(nrm[:, :], nrm[:, :], 1e-6, None, ALU.max))
                        link(V.reciprocal(nrm[:, :], nrm[:, :]))
                        att3 = att[:, :].rearrange("p (h e) -> p h e", e=HD)
                        V.tensor_tensor(att3, att3, nrm[:, :].unsqueeze(2).to_broadcast([P, HEADS, HD]), ALU.mult).then_inc(a1["att"], 1)
                        yield
                        dve.wait_ge(a1["o_ps"], u + 1)
                        t = c * CH + (s * TPS + j) * D
                        V.tensor_tensor(X[:, t:t + D], ps[:, 1, 0:D], X[:, t:t + D], ALU.add).then_inc(a1["x"], 1)
                        dve.wait_ge(a1["x"], u + 1)
                        yield

            def main(s):
                n, e = divmod(s, E)
                if s < SLOTS:
                    dve.wait_ge(g_ready, HC * (s + 1))
                    if s % GQ == 0:
                        dve.wait_ge(bc_in[s // GQ % 2], 16 * (s // GQ // 2 + 1))
                    if s >= RING_HW:
                        dve.wait_ge(slot_done, s - RING_HW + 1)
                    V.tensor_tensor(hw[:, s % RING_HW, :, :], g[:, s % 2, :, :],
                                    bc[:, s // GQ % 2, s % GQ, :].unsqueeze(1).to_broadcast([P, HC, CH]), ALU.mult).then_inc(hw_ready, 1)

            def wt(l, c):
                for r in range(WROUNDS):
                    dve.wait_ge(wt_ps, r + 1)
                    b = ps[:, r % 3, :]
                    if r < 4:
                        q = slice(r * CH, (r + 1) * CH)
                        link(V.tensor_copy(weh[:, q], b))
                        V.tensor_tensor(wel[:, q], b, weh[:, q].bitcast(f32), ALU.subtract).then_inc(wt_done, 1)
                    elif r == 4:
                        link(V.tensor_copy(qkv1h[:, :], b[:, 0:3 * P]))
                        V.tensor_tensor(qkv1l[:, :], b[:, 0:3 * P], qkv1h[:, :].bitcast(f32), ALU.subtract)
                        V.tensor_copy(woT[:, :], b[:, 3 * P:4 * P]).then_inc(wt_done, 1)
                    else:
                        link(V.tensor_copy(gth[:, 0:E], b[:, 0:E]))
                        V.tensor_tensor(gtl[:, 0:E], b[:, 0:E], gth[:, 0:E].bitcast(f32), ALU.subtract).then_inc(wt_done, 1)
                    yield

            def be(l, c):
                dve.wait_ge(w_in["be"], 32)
                link(V.tensor_copy(ber[:, :], be_raw))
                link(V.tensor_tensor(be_raw, be_raw, ber[:, :].bitcast(f32), ALU.subtract))
                link(V.tensor_scalar(ber[:, :], ber[:, :].bitcast(f32), ident[0:2, 0:1], None, ALU.mult))
                link(V.scalar_tensor_tensor(ber[:, :], be_raw, ident[0:2, 1:2], ber[:, :].bitcast(f32), ALU.mult, ALU.add))
                V.memset(kvs[:, :, :], 0.0).then_inc(be_done, 1)
                yield

            drive(main, sides({"ln": ln, "rt": rt, "ct": ct, "c0": c0, "a0": a0_, "f1": f1_, "a1": a1_, "wt": wt, "be": be}))

        @block.tensor
        def _(pe):
            T = nc.tensor

            def mm3(dst, wh, wl, xh, xl, stop=True):
                T.matmul(dst, wh, xh, start=True, stop=False)
                T.matmul(dst, wh, xl, start=False, stop=False)
                return T.matmul(dst, wl, xh, start=False, stop=stop)

            pe.wait_ge(const_ready, 1)
            pe.wait_ge(w_in["small"], 16 * 11)
            T.transpose(py[:, 0:E * HC], b1row[:, :], ident[0:E * HC, 0:E * HC]).then_inc(b1_ps, 1)

            def ln(l, c):
                yield
                yield
                pe.wait_ge(SG["xn"], nth_side("xn", l, c))
                for j in range(TPC):
                    ins = T.transpose(ps[:, 0, j * P:(j + 1) * P], xn[:, j * D:(j + 1) * D], ident[:, :])
                ins.then_inc(SG["xt_ps"], 1)
                yield

            def rt(l, c):
                pe.wait_ge(SG["xl"], nth_side("xl", l, c))
                hi, lo = split_dst(l, c)
                rh, rl = (wrh, wrl) if moe0(l) else (gth, gtl)
                if l == MOE0_A and c == 0:
                    pe.wait_ge(prep_v, 1)
                mm3(ps[:, 1, :], rh[:, :], rl[:, :], hi, lo).then_inc(SG["lgt_ps"], 1)
                yield
                pe.wait_ge(SG["lgt"], nth_side("lgt", l, c))
                for j in range(TPC):
                    ins = T.transpose(ps[:, 2, j * E:(j + 1) * E], lgT[:, j * P:(j + 1) * P], ident[0:E, 0:E])
                ins.then_inc(SG["lg_ps"], 1)
                yield
                yield

            def ct(l, c):
                pe.wait_ge(SG["comb"], nth_side("comb", l, c))
                for j in range(TPC):
                    ins = T.transpose(ps[0:E, 1, j * P:(j + 1) * P], comb[:, j, :], ident[:, :])
                ins.then_inc(SG["ct_ps"], 1)
                yield

            def c0(l, c):
                pe.wait_ge(y_out, nth(l, c) + 1)
                for j in range(TPC):
                    ins = T.transpose(ps[:, 0, j * P:(j + 1) * P], ysb[:, j * P:(j + 1) * P], ident[:, :])
                ins.then_inc(SG["yt_ps"], 1)
                yield

            def a0_(l, c):
                pe.wait_ge(SG["xl"], nth_side("xl", l, c))
                for i, (n, b) in enumerate((("q_ps", 1), ("k_ps", 2), ("v_ps", 0))):
                    w = slice(i * P, (i + 1) * P)
                    mm3(ps[:, b, :], qkv0h[:, w], qkv0l[:, w], xsh[:, :], xsl[:, :]).then_inc(a0[n], 1)
                yield
                yield
                pe.wait_ge(a0["vz"], c + 1)
                for j in range(TPC):
                    d = ps[:, 1, j * D:(j + 1) * D]
                    T.matmul(d, vv[:, j * P:(j + 1) * P], wos[:, :], start=True, stop=False)
                    ins = T.matmul(d, ones[0:1, :], bos[:, :], start=False, stop=True)
                ins.then_inc(a0["o_ps"], 1)
                yield

            def f1_(l, c):
                pe.wait_ge(SG["comb"], nth_side("comb", l, c))
                pe.wait_ge(be_done, 1)
                for j in range(TPC):
                    for q in range(E // 4):
                        u = c * TPC * 4 + 4 * j + q
                        if 4 * j + q >= 3:
                            pe.wait_ge(f1[l]["relu"], u - 2)
                        t = slice(j * P, (j + 1) * P)
                        w = slice(q * CH, (q + 1) * CH)
                        b = ps[:, u % 3, :]
                        T.matmul(b, xsh[:, t], weh[:, w], start=True, stop=False)
                        T.matmul(b, xsl[:, t], weh[:, w], start=False, stop=False)
                        T.matmul(b, xsh[:, t], wel[:, w], start=False, stop=False)
                        T.matmul(b, ones2[:, :], ber[:, w], start=False, stop=True).then_inc(f1[l]["y_ps"], 1)
                    yield

            def a1_(l, c):
                pe.wait_ge(SG["xl"], nth_side("xl", l, c))
                for s in range(NSEQ):
                    for j in range(TPS):
                        u = (c * NSEQ + s) * TPS + j
                        t = slice((s * TPS + j) * P, (s * TPS + j + 1) * P)
                        if u:
                            pe.wait_ge(a1["min"], u)
                        if s and j == 0:
                            pe.wait_ge(a1["x"], u)
                        b = ps[:, 1, 0:3 * P]
                        T.matmul(b, xsh[:, t], qkv1h[:, :], start=True, stop=False)
                        T.matmul(b, xsl[:, t], qkv1h[:, :], start=False, stop=False)
                        T.matmul(b, xsh[:, t], qkv1l[:, :], start=False, stop=True).then_inc(a1["qkv_ps"], 1)
                        yield
                    for j in range(TPS):
                        u = (c * NSEQ + s) * TPS + j
                        pe.wait_ge(a1["kv"], (c * NSEQ + s) * TPS + TPS)
                        if j:
                            pe.wait_ge(a1["x"], u)
                        for b in range(3):
                            for i in range(j + 1):
                                if b < 2:
                                    dst, r = ps[:, b, :], kvo[:, i, b * CH:(b + 1) * CH]
                                else:
                                    dst, r = ps[:, 2, 0:P], qk[:, i, P:2 * P]
                                ins = T.matmul(dst, (tri if i == j else ones)[:, :], r, start=i == 0, stop=i == j)
                        ins.then_inc(a1["cum_ps"], 1)
                        yield
                        pe.wait_ge(a1["att"], u + 1)
                        T.transpose(ps[:, 2, 0:P], att[:, :], ident[:, :]).then_inc(a1["at_ps"], 1)
                        pe.wait_ge(a1["at"], u + 1)
                        T.matmul(ps[:, 1, 0:D], attT[:, :], woT[:, :], start=True, stop=True).then_inc(a1["o_ps"], 1)
                        yield

            def main(s):
                n, e = divmod(s, E)
                if s == 0:
                    pe.wait_ge(prep_v, 3)
                if s == HALF:
                    pe.wait_ge(prep_v, 4)
                if s < SLOTS:
                    if s >= 2:
                        pe.wait_ge(g_ready, HC * (s - 1))
                    if e == 0:
                        pe.wait_ge(SG["xl"], nth_side("xl", (MOE0_A, MOE0_B)[n // NCH], n % NCH))
                    xc = col(n % NCH)
                    for h in range(HC):
                        w = slice(e * H + h * P, e * H + (h + 1) * P)
                        mm3(ph[:, s % 2, h, :], w1h[:, w], w1l[:, w], xbh[:, xc], xbl[:, xc]).then_inc(h_ready, 1)
                s2 = s - LAG
                if s2 >= 0:
                    n2, e2 = divmod(s2, E)
                    pe.wait_ge(hw_ready, s2 + 1)
                    if s2 == 0:
                        pe.wait_ge(w_in["w2"], 32)
                        pe.wait_ge(b1_ready, 1)
                    if e2 == 0 and n2:
                        pe.wait_ge(y_out, n2)
                    for h in range(HC):
                        w = slice((e2 * HC + h) * D, (e2 * HC + h + 1) * D)
                        ins = T.matmul(py[:, :], w2s[:, w], hw[:, s2 % RING_HW, h, :], start=e2 == 0 and h == 0, stop=False)
                    ins.then_inc(slot_done, 1)
                    if e2 == E - 1:
                        T.matmul(py[:, :], b2s[:, :], combT[:, col(n2 % NCH)], start=False, stop=True).then_inc(y_ready, 1)

            def wt(l, c):
                pe.wait_ge(w_in["we"], 16)
                pe.wait_ge(w_in["l1"], 16 * 5)
                pe.wait_ge(SG["ct"], 2)
                for r in range(WROUNDS):
                    if r >= 3:
                        pe.wait_ge(wt_done, r - 2)
                    if r < 5:
                        for i in range(4):
                            ins = T.transpose(ps[:, r % 3, i * P:(i + 1) * P], stage[:, (4 * r + i) * P:(4 * r + i + 1) * P], ident[:, :])
                    else:
                        ins = T.transpose(ps[:, r % 3, 0:E], stage[0:E, E * D + 4 * P:E * D + 5 * P], ident[0:E, 0:E])
                    ins.then_inc(wt_ps, 1)
                    yield

            def be(l, c):
                pe.wait_ge(wt_done, WROUNDS)
                yield

            drive(main, sides({"ln": ln, "rt": rt, "ct": ct, "c0": c0, "a0": a0_, "f1": f1_, "a1": a1_, "wt": wt, "be": be}))


_INS = ["L0_attn_x", "L0_attn_wq", "L0_attn_bq", "L0_attn_wk", "L0_attn_bk", "L0_attn_wv", "L0_attn_bv", "L0_attn_wo",
        "L0_attn_bo", "L0_ffn_Wr", "L0_ffn_br", "L0_ffn_W1", "L0_ffn_b1", "L0_ffn_W2", "L0_ffn_b2", "L1_attn_Wq",
        "L1_attn_Wk", "L1_attn_Wv", "L1_attn_Wo", "L1_ffn_gate_w", "L1_ffn_expert_w", "L1_ffn_expert_b"]


def kernel(**inputs):
    import numpy as _np
    import concourse.bacc as _bacc
    from concourse import mybir as _mybir
    from concourse.bass_utils import run_bass_kernel_spmd as _run

    nc = _bacc.Bacc("TRN2", target_bir_lowering=False, num_devices=1)
    arrays, args = {}, []
    for name in _INS:
        a = _np.ascontiguousarray(inputs[name])
        arrays[f"in_{name}_dram"] = a
        args.append(nc.dram_tensor(f"in_{name}_dram", a.shape, _mybir.dt.from_np(a.dtype), kind="ExternalInput").ap())
    shape = inputs["L0_attn_x"].shape
    args.append(nc.dram_tensor("out_0_dram", shape, _mybir.dt.float32, kind="ExternalOutput").ap())
    build_program(nc, *args)
    r = _run(nc, [arrays], core_ids=[0])
    return r.results[0]["out_0_dram"]
```
